# Optimizing a Trainium2 kernel written in Bass

```python
import numpy as np
import jax
import jax.numpy as jnp

def _softmax(x, axis=-1):
    return jax.nn.softmax(x, axis=axis)
def _gelu(x):
    return jax.nn.gelu(x, approximate=True)
def _silu(x):
    return jax.nn.silu(x)
def _sigmoid(x):
    return jax.nn.sigmoid(x)
def _layernorm(x, axis=-1, eps=1e-5):
    m = jnp.mean(x, axis=axis, keepdims=True)
    v = jnp.var(x, axis=axis, keepdims=True)
    return (x - m) / jnp.sqrt(v + eps)
def _scatter_add(tgt, idx, src, axis=0):
    return tgt.at[idx].add(src)
def _segment_sum(src, seg, n):
    return jax.ops.segment_sum(src, seg, n)

kernel_name = 'mk_conv_preact_d1_conv_nchw16_83440a'

def setup_inputs(seed: int = 0):
    np.random.seed(seed)
    _w = jnp.asarray
    def _rec_inputs():
        import jax
        import jax.numpy as jnp
        _gk = jax.random.key(seed)
        x = -7.109e-05 + 0.9999 * jax.random.normal(jax.random.fold_in(_gk, 1), (1, 16, 2048, 2048), jnp.float32)
        return x
    x = _rec_inputs()
    def _L0_conv_setup():
        import jax, jax.numpy as jnp
        import numpy as np
        N = 2048
        IN_DIM = 16
        OUT_DIM = 16

        def _set_partitions(items):
            if not items:
                yield []
                return
            first, rest = (items[0], items[1:])
            for part in _set_partitions(rest):
                for i in range(len(part)):
                    yield (part[:i] + [part[i] + [first]] + part[i + 1:])
                yield ([[first]] + part)

        def _partitions():
            items = [('i', 0), ('i', 1), ('o', 0), ('o', 1)]
            parts = []
            for p in _set_partitions(items):
                blocks = []
                for blk in p:
                    iset = sorted((d for t, d in blk if t == 'i'))
                    oset = sorted((d for t, d in blk if t == 'o'))
                    blocks.append((iset, oset))
                parts.append(blocks)
            return parts
        PARTITIONS = _partitions()

        def _basis_apply(X, W, blocks, eye_n, ones_n):
            blk_letters = 'ijkl'
            in_sub = [''] * 2
            for bi, (iset, oset) in enumerate(blocks):
                for d in iset:
                    in_sub[d] = blk_letters[bi]
            subs = ['bc' + ''.join(in_sub)]
            ops = [X]
            fresh = iter('uvwxyz')
            out_letter = [''] * 2
            denom = 1.0
            for bi, (iset, oset) in enumerate(blocks):
                if not oset:
                    denom *= float(N)
                    continue
                if iset:
                    base = blk_letters[bi]
                else:
                    base = next(fresh)
                    subs.append(base)
                    ops.append(ones_n)
                out_letter[oset[0]] = base
                for od in oset[1:]:
                    l2 = next(fresh)
                    subs.append(base + l2)
                    ops.append(eye_n)
                    out_letter[od] = l2
            subs.append('co')
            ops.append(W)
            expr = ','.join(subs) + '->bo' + ''.join(out_letter)
            return jnp.einsum(expr, *ops) / denom
        key = jax.random.key(seed)
        k1, k2 = jax.random.split(key)
        stdv = 0.1 / np.sqrt(IN_DIM)
        X = jax.random.normal(k1, (1, IN_DIM, N, N), dtype=jnp.float32)
        weights = jax.random.uniform(k2, (len(PARTITIONS), IN_DIM, OUT_DIM), minval=-stdv, maxval=stdv, dtype=jnp.float32)
        bias = jnp.ones((len(PARTITIONS),), dtype=jnp.float32)
        return {'X': X, 'weights': weights, 'bias': bias}
    _L0_conv_all = _L0_conv_setup()
    _L0_conv_in = {k: v for k, v in _L0_conv_all.items() if k in ('weights', 'bias', )}
    del _L0_conv_all

    return {
        "x": x,
        "L0_conv_weights": _L0_conv_in["weights"],
        "L0_conv_bias": _L0_conv_in["bias"],
    }

def reference(x, L0_conv_weights, L0_conv_bias):
    import jax
    import jax.numpy as jnp
    def _L0_conv_ref(X, weights, bias):
        import jax, jax.numpy as jnp
        import numpy as np
        N = 2048
        IN_DIM = 16
        OUT_DIM = 16

        def _set_partitions(items):
            if not items:
                yield []
                return
            first, rest = (items[0], items[1:])
            for part in _set_partitions(rest):
                for i in range(len(part)):
                    yield (part[:i] + [part[i] + [first]] + part[i + 1:])
                yield ([[first]] + part)

        def _partitions():
            items = [('i', 0), ('i', 1), ('o', 0), ('o', 1)]
            parts = []
            for p in _set_partitions(items):
                blocks = []
                for blk in p:
                    iset = sorted((d for t, d in blk if t == 'i'))
                    oset = sorted((d for t, d in blk if t == 'o'))
                    blocks.append((iset, oset))
                parts.append(blocks)
            return parts
        PARTITIONS = _partitions()

        def _basis_apply(X, W, blocks, eye_n, ones_n):
            blk_letters = 'ijkl'
            in_sub = [''] * 2
            for bi, (iset, oset) in enumerate(blocks):
                for d in iset:
                    in_sub[d] = blk_letters[bi]
            subs = ['bc' + ''.join(in_sub)]
            ops = [X]
            fresh = iter('uvwxyz')
            out_letter = [''] * 2
            denom = 1.0
            for bi, (iset, oset) in enumerate(blocks):
                if not oset:
                    denom *= float(N)
                    continue
                if iset:
                    base = blk_letters[bi]
                else:
                    base = next(fresh)
                    subs.append(base)
                    ops.append(ones_n)
                out_letter[oset[0]] = base
                for od in oset[1:]:
                    l2 = next(fresh)
                    subs.append(base + l2)
                    ops.append(eye_n)
                    out_letter[od] = l2
            subs.append('co')
            ops.append(W)
            expr = ','.join(subs) + '->bo' + ''.join(out_letter)
            return jnp.einsum(expr, *ops) / denom
        eye_n = jnp.eye(N, dtype=X.dtype)
        ones_n = jnp.ones((N,), dtype=X.dtype)
        Y = None
        for i, blocks in enumerate(PARTITIONS):
            Yi = _basis_apply(X, weights[i], blocks, eye_n, ones_n)
            Y = Yi if Y is None else Y + Yi
        return Y + jnp.sum(bias)

    def _gn(v, G=8, eps=1e-5):
        B_, C_, H_, W_ = v.shape
        g = v.reshape(B_, G, C_ // G, H_, W_)
        m = jnp.mean(g, axis=(2, 3, 4), keepdims=True)
        s = jnp.var(g, axis=(2, 3, 4), keepdims=True)
        return ((g - m) / jnp.sqrt(s + eps)).reshape(v.shape)

    def _ln_c(v, eps=1e-6):
        m = jnp.mean(v, axis=1, keepdims=True)
        s = jnp.var(v, axis=1, keepdims=True)
        return (v - m) / jnp.sqrt(s + eps)

    def _ln_t(v, eps=1e-5):
        m = jnp.mean(v, axis=-1, keepdims=True)
        s = jnp.var(v, axis=-1, keepdims=True)
        return (v - m) / jnp.sqrt(s + eps)

    def _to_tokens(v):
        B_, C_, H_, W_ = v.shape
        return v.reshape(B_, C_, H_ * W_).transpose(0, 2, 1)
    def _from_tokens(t, like):
        B_, C_, H_, W_ = like.shape
        return t.transpose(0, 2, 1).reshape(B_, C_, H_, W_)

    x = x + _L0_conv_ref(_gn(x), L0_conv_weights, L0_conv_bias)
    return x


_drawn_inputs = setup_inputs


def setup_inputs(seed=0):
    import zlib

    import numpy as np

    out = dict(_drawn_inputs(seed))
    spreads = {'L0_conv_bias': (1.0, 0.2)}
    factors = {'L0_conv_weights': 6.774}
    for name, (base, spread) in spreads.items():
        noise = np.random.default_rng([zlib.crc32(name.encode()), seed]).standard_normal(out[name].shape)
        drawn = base * np.exp(spread * noise) if base else spread * noise
        out[name] = jnp.asarray(drawn.astype(out[name].dtype))
    for name, factor in factors.items():
        out[name] = (out[name] * factor).astype(out[name].dtype)
    return out
```

```python
from contextlib import ExitStack

import numpy as np

import concourse.bass as bass
from concourse import mybir
from concourse.alu_op_type import AluOpType as ALU

F32 = mybir.dt.float32
BF16 = mybir.dt.bfloat16
ACT = mybir.ActivationFunctionType
AX_X = mybir.AxisListType.X

P = 128
C = 16
N = 2048
GROUPS = 8
EPS = 1e-5
BANK = 512

ROWS1 = P // C
TILES1 = N // ROWS1
RING1 = 8
PE_COLS = 2 * BANK
POOL_COLS = N - PE_COLS

Q = 4
H = C * Q
B = 256
NB = N // B
M_BLOCK = B // Q
M_UNIT = 8
UNIT = M_UNIT * B
UNITS = M_BLOCK // M_UNIT
PIECE = 2 * UNIT
PIECES = UNITS // 2
SB = B // 32
C8 = C // 2
BLOCKS = NB + NB * (NB - 1) // 2
DIAG_BLOCKS = NB
ROWS_PIECE = 2 * M_UNIT * Q
FREE = 2
LEAD = 3
PIECE_DMAS = Q * 16
ALL_DIAGONAL = DIAG_BLOCKS * PIECES // 2 * PIECE_DMAS
STRIP_DMAS = SB * 2 * 16
DIAG_STRIP_DMAS = (SB - ROWS_PIECE // 32) * 2 * 16

V_DIAG, V_ROW, V_COL, VP = 0, 32, 64, 96

W_DIRECT, W_TURNED = 8, 6
FEEDS = {
    "A": (5, 12, 7),
    "B": (9, 13, 10),
    "D": (0, 3, 1),
    "K": (11, 14, W_DIRECT),
    "K2": (None, None, W_TURNED),
    "DK": (2, 4, None),
}
SLOTS = list(FEEDS)
SMALL_DMAS = sum(w is not None for f in FEEDS.values() for w in f) + 4 * Q + 1

CONSTS = {"diag_rows": VP, "mean_rows": VP, "column_rows": VP, "none": VP, "group": P, "to_vectors": VP, "to_halves": P,
          "eye": P, "spread": P, "mask": Q, "mask8": ROWS1, "unit": 1}
CONST_COLS = sum(CONSTS.values())


def constants():
    p = np.arange(P)
    c1 = p // ROWS1
    out = {k: np.zeros((P, n), np.float32) for k, n in CONSTS.items()}
    per = P // GROUPS
    out["group"][:] = (p[:, None] // per == p[None, :] // per) / per
    for c in range(C):
        mine = c1 == c
        out["diag_rows"][mine, V_DIAG + c] = 1.0
        out["mean_rows"][mine, V_ROW + c] = 1.0
        out["column_rows"][mine, V_COL + c] = 1.0
        for base in (V_DIAG, V_ROW, V_COL):
            out["to_vectors"][c * ROWS1, base + c] = 1.0
        for half in range(2):
            out["to_halves"][c * ROWS1, half * H + c * Q:half * H + (c + 1) * Q] = 1.0
    out["eye"][p, p] = 1.0
    for part in range(3):
        for which in range(2):
            for o in range(C):
                row = 32 * part + C * which + o
                out["spread"][row, which * H + o * Q:which * H + (o + 1) * Q] = 1.0
    out["mask"][p, p % Q] = 1.0
    out["mask8"][p, p % ROWS1] = 1.0
    out["unit"][:] = 1.0
    out["unit"][V_COL:V_COL + C] = 1.0 / N
    return np.concatenate([out[k] for k in CONSTS], 1)


def program(nc, x, weights, bias, consts, out):
    with ExitStack() as ctx:
        def sb(name, shape, dt=F32):
            return ctx.enter_context(nc.sbuf_tensor(name, shape, dt))

        def sem(name):
            return ctx.enter_context(nc.semaphore(name))

        turned_in = sb("turned_in", [P, SB * C8 * B])
        turned_out = sb("turned_out", [P, SB * C8 * B])
        mixed_in = sb("mixed_in", [P, 2, PIECE])
        result = sb("result", [P, 2 * PIECE + B])
        psum = ctx.enter_context(nc.psum_tensor("psum", [P, 8, BANK], F32))

        mix = sb("mix", [P, P])
        spread = sb("spread", [P, P], BF16)
        along = sb("along", [VP, N], BF16)
        per_row = sb("per_row", [P, N // Q])
        on_diag = sb("on_diag", [H, N // Q])
        along_now = sb("along_now", [VP, 2, B], BF16)
        per_row_now = sb("per_row_now", [P, 2, M_BLOCK])
        mask = sb("mask", [P, Q])
        small = sb("small", [P, 64])
        diag_add = sb("diag_add", [H, M_UNIT, Q])

        tiles = turned_out[:, :].rearrange("p (k n) -> p k n", k=RING1)
        masked_diag = result[:, 0:N]
        masked_mean = result[:, N:2 * N]
        work = result[:, 2 * N:3 * N]
        pool_sum = work[:, 0:POOL_COLS]
        row_stats = work[:, 1024:1536].rearrange("p (t k) -> p t k", k=2)
        chunk_stats = work[:, 1536:1536 + RING1 * 24].rearrange("p (k j f) -> p k j f", k=RING1, f=6)
        ring_stats = work[:, 1792:1792 + 2 * RING1].rearrange("p (k f) -> p k f", f=2)
        vec = turned_out[0:VP, 0:N]
        full = turned_out[0:VP, N:2 * N]
        middle = turned_out[0:VP, 2 * N:2 * N + N // 2].bitcast(BF16)
        at = 3 * N
        const = {}
        for k, n in CONSTS.items():
            const[k] = result[:, at:at + n]
            at += n
        all_consts = result[:, 3 * N:at]

        def table(rows, n):
            nonlocal at
            at += n
            assert at <= 2 * PIECE + B
            return result[0:rows, at - n:at]

        row_mix = table(VP, Q * P).rearrange("p (q n) -> p q n", q=Q)
        diag_mix = table(VP, Q * H).rearrange("p (q n) -> p q n", q=Q)
        along_mix = work[0:VP, 1824:1824 + VP]
        const_mix = table(VP, P)
        const_diag_mix = table(VP, H)
        w_vec = table(VP, len(SLOTS) * C).rearrange("p (k o) -> p k o", o=C)
        w_lower = table(P, C)
        w_upper = table(P, C)
        ones_row = table(P, P)
        bias_col = table(P, 1)

        def col(n, rows=P, width=1, base=0):
            return small[base:base + rows, n:n + width]

        psum_flat = psum[:, :, :].rearrange("p b n -> p (b n)")

        tile_loaded = [sem(f"tile_loaded{k}") for k in range(RING1)]
        rows_read, cols_read, pool_read = sem("rows_read"), sem("cols_read"), sem("pool_read")
        pool_cleared = sem("pool_cleared")
        rows_merged, rows_kept = sem("rows_merged"), sem("rows_kept")
        consts_loaded, weights_loaded = sem("consts_loaded"), sem("weights_loaded")
        zeroed = sem("zeroed")
        dve_step = sem("dve_step")
        vectors_masked, vectors_summed, full_copied = sem("vectors_masked"), sem("vectors_summed"), sem("full_copied")
        along_ready = sem("along_ready")
        mean_ready, mean_summed, spread_ready, var_summed = sem("mean_ready"), sem("mean_summed"), sem("spread_ready"), sem("var_summed")
        var_ready, std_ready, scale_ready, scale_moved = sem("var_ready"), sem("std_ready"), sem("scale_ready"), sem("scale_moved")
        vectors_ready, tables_summed, setup_done = sem("vectors_ready"), sem("tables_summed"), sem("setup_done")
        scale_kept, means_ready = sem("scale_kept"), sem("means_ready")
        turned_loaded = [sem(f"turned_loaded{k}") for k in range(2)]
        direct_loaded = [sem(f"direct_loaded{k}") for k in range(2)]
        turned_ready, mixed, evacuated, taken = sem("turned_ready"), sem("mixed"), sem("evacuated"), sem("taken")
        bias_ready, diag_masked = sem("bias_ready"), sem("diag_masked")
        direct_stored = [sem(f"direct_stored{k}") for k in range(2)]
        diagonal_stored = [sem(f"diagonal_stored{k}") for k in range(2)]
        turned_stored = [sem(f"turned_stored{k}") for k in range(2)]

        x_m = x.rearrange("c (m q) s -> c m q s", q=Q)
        out_m = out.rearrange("c (m q) s -> c m q s", q=Q)

        def block_of(p):
            return p & (NB - 1), (p + (p >> 3)) & (NB - 1)

        def place(eng, p):
            return tuple(z if isinstance(z, int) else eng.snap(eng.to_reg(z)) for z in block_of(p))

        def half_of(par):
            return H if par == 0 else 0

        def first_col(diag, kk):
            return kk * ROWS_PIECE if diag else 0

        def direct_dram(t, at_block, kk, rr, diag):
            r, s = at_block
            c0 = first_col(diag, kk)
            return t[:, bass.ds(r * M_BLOCK + kk * 2 * M_UNIT, 2 * M_UNIT), rr, bass.ds(s * B + c0, B - c0)]

        def piece_side(t, kk, rr, diag):
            slot = kk % 2
            v = t[rr:H:Q, slot * PIECE:(slot + 1) * PIECE].rearrange("p (m s) -> p m s", s=B)
            return v[:, :, first_col(diag, kk):]

        def strip_width(diag, b, own):
            return (b * 32 // ROWS_PIECE + own) * ROWS_PIECE if diag else B

        def turned_dram(t, at_block, b, h, width):
            r, s = at_block
            return t[h * C8:(h + 1) * C8, bass.ds(s * B + b * 32, 32), bass.ds(r * B, width)].rearrange("c s r -> s c r")

        def strip_side(t, par, b, h, width):
            lo = half_of(par) + 32 * h
            return t[lo:lo + 32, b * C8 * B:(b + 1) * C8 * B].rearrange("p (c r) -> p c r", c=C8)[:, :, 0:width]

        def unit_strips(t, par, k, b0):
            lo = half_of(par)
            v = t[lo:lo + H, :].rearrange("p (b c r) -> p b c r", b=SB, c=C8)
            return v[:, b0:, :, k * M_UNIT * Q:(k + 1) * M_UNIT * Q].rearrange("p b c (m q) -> p m b c q", q=Q)

        def unit_side(t, k, c0):
            lo = unit_cols(k)
            return t[H:P, lo:lo + UNIT].rearrange("p (m s) -> p m s", s=B)[:, :, c0:]

        mixed_flat = mixed_in[:, :, :].rearrange("p k n -> p (k n)")

        def unit_cols(k):
            return ((k // 2) % 2) * PIECE + (k % 2) * UNIT

        def wait_if(eng, semaphore, value):
            if not isinstance(value, int) or value > 0:
                eng.wait_ge(semaphore, value)

        def store_piece(eng, at_block, kk, diag):
            stored = diagonal_stored if diag else direct_stored
            for rr in range(Q):
                eng.dma_start(direct_dram(out_m, at_block, kk, rr, diag),
                              piece_side(result, kk, rr, diag)).then_inc(stored[kk % 2], 16)

        block = ctx.enter_context(nc.Block())

        @block.sync
        def _(sp):
            def load_tile(t, k):
                sp.dma_start(tiles[:, k, :], x[:, bass.ds(t * ROWS1, ROWS1), :]).then_inc(tile_loaded[k], 16)

            load_tile(0, 0)
            sp.dma_start(all_consts, consts).then_inc(consts_loaded, 16)
            for k in range(1, RING1):
                load_tile(k, k)
            with sp.Fori(0, TILES1 // RING1 - 1) as i:
                for k in range(RING1):
                    sp.wait_ge(rows_read, i * RING1 + (k + 1))
                    sp.wait_ge(cols_read, i * RING1 + (k + 1))
                    sp.wait_ge(pool_read, i * RING1 + (k + 1))
                    load_tile(i * RING1 + (RING1 + k), k)

            def load_piece(at_block, kk, diag):
                for rr in range(Q):
                    sp.dma_start(piece_side(mixed_flat, kk, rr, diag),
                                 direct_dram(x_m, at_block, kk, rr, diag)).then_inc(direct_loaded[kk % 2], 16)

            def load_strips(at_block, par, bs, diag):
                for b in bs:
                    w = strip_width(diag, b, 1)
                    for h in range(2):
                        sp.dma_start(strip_side(turned_in, par, b, h, w), turned_dram(x, at_block, b, h, w)).then_inc(turned_loaded[par], 16)

            first = block_of(0)
            load_strips(first, 0, range(SB), True)
            load_piece(first, 0, True)
            load_piece(first, 1, True)
            load_strips(block_of(1), 1, range(SB), True)

            def block_loads(p, par, diag=False, next_diag=False, last=False):
                here, following = place(sp, p), None if last else place(sp, p + 1)
                ahead = not last and not (isinstance(p, int) and p == 0)
                if ahead:
                    wait_if(sp, turned_ready, p * UNITS)
                for kk in range(PIECES):
                    if ahead and kk < 2:
                        load_strips(following, 1 - par, range(4 * kk, 4 * kk + 4), next_diag)
                    if last and kk >= 2:
                        continue
                    sp.wait_ge(mixed, p * UNITS + (2 * kk + 2))
                    if kk < 2:
                        load_piece(here, kk + 2, diag)
                    else:
                        load_piece(following, kk - 2, next_diag)

            block_loads(0, 0, True, True)
            block_loads(1, 1, True, True)
            with sp.Fori(1, DIAG_BLOCKS // 2 - 1) as i:
                block_loads(i * 2, 0, True, True)
                block_loads(i * 2 + 1, 1, True, True)
            block_loads(DIAG_BLOCKS - 2, 0, True, True)
            block_loads(DIAG_BLOCKS - 1, 1, True)
            with sp.Fori(DIAG_BLOCKS // 2, BLOCKS // 2 - 1) as i:
                block_loads(i * 2, 0)
                block_loads(i * 2 + 1, 1)
            block_loads(BLOCKS - 2, 0)
            block_loads(BLOCKS - 1, 1, last=True)

        @block.gpsimd
        def _(pool):
            nc.gpsimd.memset(pool_sum, 0.0).then_inc(pool_cleared, 1)
            pool.wait_ge(pool_cleared, 1)

            def sum_columns(i):
                for k in range(RING1):
                    pool.wait_ge(tile_loaded[k], i * 16 + 16)
                    wait_if(pool, pool_read, i * RING1 + k)
                    nc.gpsimd.tensor_tensor(pool_sum, pool_sum, tiles[:, k, PE_COLS:N], ALU.add).then_inc(pool_read, 1)

            sum_columns(0)
            with pool.Fori(1, TILES1 // RING1) as i:
                sum_columns(i)

            def store_strips(at_block, par, bs, diag):
                for b in bs:
                    w = strip_width(diag, b, 0)
                    if w == 0:
                        continue
                    for h in range(2):
                        pool.dma_start(turned_dram(out, at_block, b, h, w), strip_side(turned_out, par, b, h, w)).then_inc(turned_stored[par], 16)

            def diagonal_block_stores(p, par):
                here = place(pool, p)
                pool.wait_ge(taken, p * UNITS + (UNITS + FREE))
                store_strips(here, par, range(SB), True)

            def block_stores(p, par, first=False):
                here = place(pool, p)
                if not first:
                    behind = place(pool, p - 1)
                    pool.wait_ge(taken, p * UNITS + FREE)
                for kk in range(PIECES):
                    if not first:
                        store_strips(behind, 1 - par, range(3 * kk, min(3 * kk + 3, SB)), False)
                    pool.wait_ge(evacuated, p * UNITS + (2 * kk + 2 + FREE))
                    store_piece(pool, here, kk, False)

            with pool.Fori(0, DIAG_BLOCKS // 2) as i:
                diagonal_block_stores(i * 2, 0)
                diagonal_block_stores(i * 2 + 1, 1)
            block_stores(DIAG_BLOCKS, 0, first=True)
            with pool.Fori(DIAG_BLOCKS // 2, BLOCKS // 2 - 1) as i:
                block_stores(i * 2 + 1, 1)
                block_stores(i * 2 + 2, 0)
            block_stores(BLOCKS - 1, 1)
            pool.wait_ge(taken, BLOCKS * UNITS + FREE)
            store_strips(block_of(BLOCKS - 1), 1, range(SB), False)
            for slot in range(2):
                pool.wait_ge(diagonal_stored[slot], ALL_DIAGONAL)
                pool.wait_ge(direct_stored[slot], (BLOCKS - DIAG_BLOCKS) * PIECES // 2 * PIECE_DMAS)
                pool.wait_ge(turned_stored[slot], DIAG_BLOCKS // 2 * DIAG_STRIP_DMAS + (BLOCKS - DIAG_BLOCKS) // 2 * STRIP_DMAS)

        @block.scalar
        def _(act):
            act.wait_ge(zeroed, 2)
            for slot, name in enumerate(SLOTS):
                for base, which in zip((V_DIAG, V_ROW, V_COL), FEEDS[name]):
                    if which is not None:
                        act.dma_start(w_vec[base:base + C, slot, :], weights[which]).then_inc(weights_loaded, 16)
            for half, (lower, upper) in enumerate(((W_DIRECT, W_TURNED), (W_TURNED, W_DIRECT))):
                for dst, which in ((w_lower, lower), (w_upper, upper)):
                    for rr in range(Q):
                        act.dma_start(dst[half * H + rr:(half + 1) * H:Q, :], weights[which]).then_inc(weights_loaded, 16)
            act.dma_start(bias_col[0:15, :], bias.rearrange("(p a) -> p a", a=1)).then_inc(weights_loaded, 16)

            act.wait_ge(var_ready, 1)
            nc.scalar.activation(col(9), col(8), ACT.Sqrt).then_inc(std_ready, 1)
            act.wait_ge(vectors_summed, 1)
            act.wait_ge(scale_kept, 1)
            nc.scalar.activation(vec, psum_flat[0:VP, 0:N], ACT.Identity, bias=col(19, VP), scale=col(18, VP),
                                 accum_out=col(21, VP)).then_inc(vectors_ready, 1)
            act.wait_ge(tables_summed, 1)
            for j in range(4):
                nc.scalar.copy(full[:, j * BANK:(j + 1) * BANK], psum[0:VP, j, :]).then_inc(full_copied, 1)

            def bias_slices(p, par):
                r, s = block_of(p)
                nc.scalar.copy(per_row_now[:, par, :], per_row[:, bass.ds(r * M_BLOCK, M_BLOCK)]).then_inc(bias_ready, 1)
                nc.scalar.copy(along_now[:, par, :], along[:, bass.ds(s * B, B)]).then_inc(bias_ready, 1)

            act.wait_ge(setup_done, 1)
            bias_slices(0, 0)

            def store_diagonal_piece(p, kk):
                here = place(act, p)
                act.wait_ge(taken, p * UNITS + (2 * kk + 2 + FREE))
                store_piece(act, here, kk, True)

            def evacuate_block(p, par, diag=False, first_pair=False, last=False):
                act.wait_ge(bias_ready, p * 2 + 2)
                for k in range(UNITS):
                    act.wait_ge(mixed, p * UNITS + (k + 1))
                    if k == 1 and isinstance(p, int) and p == 1:
                        act.wait_ge(along_ready, 4)
                    if k == 1 and not last:
                        act.wait_ge(evacuated, p * UNITS + FREE)
                        bias_slices(p + 1, 1 - par)
                    if k % 2 == 0:
                        slot, before = (k // 2) % 2, p * (2 * PIECE_DMAS) + (k // 4) * PIECE_DMAS
                        if diag:
                            wait_if(act, diagonal_stored[slot], before)
                        elif first_pair and k < 4:
                            act.wait_ge(diagonal_stored[slot], ALL_DIAGONAL)
                        else:
                            act.wait_ge(direct_stored[slot], before - ALL_DIAGONAL)
                        wait_if(act, taken, p * UNITS + k)
                    banks = psum[:, 4 * (k % 2):4 * (k % 2) + 4, :].rearrange("p b (m s) -> p (b m) s", s=B)
                    for m in range(M_UNIT):
                        lo, c0 = unit_cols(k) + m * B, first_col(diag, k // 2)
                        one = nc.scalar.activation(result[:, lo + c0:lo + B], banks[:, m, c0:], ACT.Identity,
                                                   bias=per_row_now[:, par, k * M_UNIT + m:k * M_UNIT + m + 1])
                    one.then_inc(evacuated, 1)
                    if diag and k % 2 == 0:
                        if k > 0:
                            store_diagonal_piece(p, k // 2 - 1)
                        elif not isinstance(p, int) or p > 0:
                            store_diagonal_piece(p - 1, PIECES - 1)

            evacuate_block(0, 0, True)
            evacuate_block(1, 1, True)
            with act.Fori(1, DIAG_BLOCKS // 2) as i:
                evacuate_block(i * 2, 0, True)
                evacuate_block(i * 2 + 1, 1, True)
            store_diagonal_piece(DIAG_BLOCKS - 1, PIECES - 1)
            evacuate_block(DIAG_BLOCKS, 0, first_pair=True)
            with act.Fori(DIAG_BLOCKS // 2, BLOCKS // 2 - 1) as i:
                evacuate_block(i * 2 + 1, 1)
                evacuate_block(i * 2 + 2, 0)
            evacuate_block(BLOCKS - 1, 1, last=True)

        @block.tensor
        def _(pe):
            pe.wait_ge(consts_loaded, 16)

            def column_sums(i, first=False):
                for k in range(RING1):
                    pe.wait_ge(tile_loaded[k], i * 16 + 16)
                    for j in range(PE_COLS // BANK):
                        one = nc.tensor.matmul(psum[0:VP, j, :], const["column_rows"], tiles[:, k, j * BANK:(j + 1) * BANK],
                                               start=(first and k == 0), stop=False, skip_group_check=True)
                    one.then_inc(cols_read, 1)

            def place_rows(i):
                pe.wait_ge(vectors_masked, i + 1)
                lo = i * (RING1 * ROWS1)
                for name, masked in (("diag_rows", masked_diag), ("mean_rows", masked_mean)):
                    nc.tensor.matmul(psum_flat[0:VP, bass.ds(lo, RING1 * ROWS1)], const[name],
                                     masked[:, bass.ds(lo, RING1 * ROWS1)], start=False, stop=False, skip_group_check=True)

            for j in range(PE_COLS // BANK, 4):
                nc.tensor.matmul(psum[0:VP, j, :], const["none"], all_consts[:, 0:BANK], start=True, stop=False,
                                 skip_group_check=True)
            column_sums(0, first=True)
            with pe.Fori(1, TILES1 // RING1) as i:
                column_sums(i)
                place_rows(i - 1)
            place_rows(TILES1 // RING1 - 1)
            pe.wait_ge(pool_read, TILES1)
            for j in range(PE_COLS // BANK, 4):
                one = nc.tensor.matmul(psum[0:VP, j, :], const["column_rows"],
                                       pool_sum[:, j * BANK - PE_COLS:(j + 1) * BANK - PE_COLS],
                                       start=False, stop=True, skip_group_check=True)
            one.then_inc(vectors_summed, 1)
            pe.wait_ge(mean_ready, 1)
            nc.tensor.matmul(psum[:, 4, 0:1], const["group"], col(0), start=True, stop=True).then_inc(mean_summed, 1)
            pe.wait_ge(spread_ready, 1)
            nc.tensor.matmul(psum[:, 5, 0:1], const["group"], col(6), start=True, stop=True).then_inc(var_summed, 1)
            pe.wait_ge(scale_ready, 1)
            nc.tensor.matmul(psum[:, 6, 0:2], const["to_halves"], col(14, width=2), start=True, stop=True)
            nc.tensor.matmul(psum[0:VP, 7, 0:2], const["to_vectors"], col(14, width=2), start=True, stop=True).then_inc(scale_moved, 1)

            pe.wait_ge(vectors_ready, 1)
            pe.wait_ge(scale_kept, 1)
            vec_m = vec.rearrange("p (m q) -> p q m", q=Q)
            for j in range(4):
                nc.tensor.matmul(psum[0:VP, j, :], along_mix, vec[:, j * BANK:(j + 1) * BANK], start=True, stop=True)
            for rr in range(Q):
                nc.tensor.matmul(psum[:, 4, :], row_mix[:, rr, :], vec_m[:, rr, :], start=(rr == 0), stop=(rr == Q - 1))
            for rr in range(Q):
                nc.tensor.matmul(psum[0:H, 5, :], diag_mix[:, rr, :], vec_m[:, rr, :], start=(rr == 0), stop=(rr == Q - 1))
            pe.wait_ge(means_ready, 1)
            nc.tensor.matmul(psum[:, 6, 0:1], const_mix, col(20, VP), start=True, stop=False)
            nc.tensor.matmul(psum[:, 6, 0:1], ones_row, bias_col, start=False, stop=True)
            nc.tensor.matmul(psum[0:H, 7, 0:1], const_diag_mix, col(20, VP), start=True, stop=True).then_inc(tables_summed, 1)

            pe.wait_ge(setup_done, 1)

            def mix_block(p, par, diag=False):
                for k in range(UNITS):
                    if k == 0:
                        pe.wait_ge(bias_ready, p * 2 + 2)
                    if k % 2 == 0:
                        pe.wait_ge(direct_loaded[(k // 2) % 2], p * (2 * PIECE_DMAS) + (k // 4 + 1) * PIECE_DMAS)
                    pe.wait_ge(turned_ready, p * UNITS + (k + 1))
                    pe.wait_ge(evacuated, p * UNITS + (k + 1))
                    c0 = first_col(diag, k // 2)
                    units_m = BANK // B
                    banks = [psum[:, 4 * (k % 2) + j, :].rearrange("p (m s) -> p m s", s=B)[:, :, c0:] for j in range(4)]
                    for j in range(4):
                        lo = unit_cols(k) + j * BANK
                        nc.tensor.matmul(banks[j], mix[:, :],
                                         mixed_flat[:, lo:lo + BANK].rearrange("p (m s) -> p m s", s=B)[:, :, c0:],
                                         start=True, stop=False, skip_group_check=True)
                    for j in range(4):
                        one = nc.tensor.matmul(banks[j], spread[0:VP, :],
                                               along_now[:, par, c0:].unsqueeze(1).to_broadcast([VP, units_m, B - c0]),
                                               start=False, stop=True, skip_group_check=True)
                    one.then_inc(mixed, 1)

            with pe.Fori(0, DIAG_BLOCKS // 2) as i:
                mix_block(i * 2, 0, True)
                mix_block(i * 2 + 1, 1, True)
            with pe.Fori(DIAG_BLOCKS // 2, BLOCKS // 2) as i:
                mix_block(i * 2, 0)
                mix_block(i * 2 + 1, 1)

        @block.vector
        def _(dve):
            v = nc.vector
            steps = [0]

            def link(ins):
                steps[0] += 1
                ins.then_inc(dve_step, 1)
                dve.wait_ge(dve_step, steps[0])

            v.memset(w_vec, 0.0).then_inc(zeroed, 1)
            v.memset(bias_col, 0.0).then_inc(zeroed, 1)
            v.memset(ones_row, 1.0)
            v.memset(diag_mix, 0.0)
            link(v.memset(row_mix, 0.0))

            dve.wait_ge(consts_loaded, 16)

            def row_statistics(i):
                for k in range(RING1):
                    dve.wait_ge(tile_loaded[k], i * 16 + 16)
                    for j in range(4):
                        v.bn_stats(chunk_stats[:, k, j, :], tiles[:, k, j * BANK:(j + 1) * BANK])
                    here = bass.ds(i * (RING1 * ROWS1) + k * ROWS1, ROWS1)
                    v.tensor_tensor(masked_diag[:, here], tiles[:, k, here], const["mask8"], ALU.mult).then_inc(rows_read, 1)
                dve.wait_ge(rows_read, i * RING1 + RING1)
                v.memset(col(63), 0.0)
                for k in range(RING1):
                    one = v.bn_aggr(ring_stats[:, k, :], chunk_stats[:, k, :, :])
                one.then_inc(rows_merged, 1)
                dve.wait_ge(rows_merged, i + 1)
                v.tensor_copy(row_stats[:, bass.ds(i * RING1, RING1), :], ring_stats[:, :, :]).then_inc(rows_kept, 1)
                v.tensor_tensor(masked_mean[:, bass.ds(i * (RING1 * ROWS1), RING1 * ROWS1)].rearrange("p (k r) -> p k r", r=ROWS1),
                                ring_stats[:, :, 0].unsqueeze(2).to_broadcast([P, RING1, ROWS1]),
                                const["mask8"].unsqueeze(1).to_broadcast([P, RING1, ROWS1]),
                                ALU.mult).then_inc(vectors_masked, 1)
                dve.wait_ge(vectors_masked, i + 1)

            row_statistics(0)

            dve.wait_ge(weights_loaded, SMALL_DMAS * 16)
            slot_of = {name: w_vec[:, n, :] for n, name in enumerate(SLOTS)}
            for rr in range(Q):
                v.tensor_copy(row_mix[:, rr, rr:H:Q], slot_of["A"])
                v.tensor_copy(row_mix[:, rr, H + rr:P:Q], slot_of["B"])
                v.tensor_copy(diag_mix[:, rr, rr:H:Q], slot_of["D"])
            for part in range(3):
                v.tensor_copy(along_mix[:, 32 * part:32 * part + C], slot_of["B"])
                v.tensor_copy(along_mix[:, 32 * part + C:32 * part + 2 * C], slot_of["A"])
            link(v.tensor_tensor(slot_of["K"], slot_of["K"], slot_of["K2"], ALU.add))
            for half in range(2):
                v.tensor_copy(const_mix[:, half * H:(half + 1) * H].rearrange("p (o q) -> p o q", q=Q),
                              slot_of["K"].unsqueeze(2).to_broadcast([VP, C, Q]))
            v.tensor_copy(const_diag_mix.rearrange("p (o q) -> p o q", q=Q),
                          slot_of["DK"].unsqueeze(2).to_broadcast([VP, C, Q]))
            v.tensor_copy(spread[:, :], const["spread"])
            link(v.tensor_copy(mask[:, :], const["mask"]))

            with dve.Fori(1, TILES1 // RING1) as i:
                row_statistics(i)

            def turn(p, par, k, diag, piece_freed=True):
                if k == 0:
                    dve.wait_ge(turned_loaded[par], p * (STRIP_DMAS // 2) + (STRIP_DMAS // 2 * (2 - par)))
                if k % 2 == 0 and piece_freed:
                    dve.wait_ge(mixed, p * UNITS + k - 2)
                c0 = first_col(diag, k // 2)
                v.transpose(unit_side(mixed_flat, k, c0).rearrange("p m (b s) -> p m b s", s=32),
                            unit_strips(turned_in, par, k, c0 // 32)).then_inc(turned_ready, 1)

            dve.wait_ge(rows_kept, TILES1 // RING1)
            link(v.bn_stats(col(24, width=6), row_stats[:, :, 0]))
            link(v.bn_aggr(col(0, width=2), col(24, width=6)))
            link(v.tensor_reduce(col(2), row_stats[:, :, 1], AX_X, ALU.add))
            link(v.scalar_tensor_tensor(col(3), col(2), 1.0 / TILES1, col(1), ALU.mult, ALU.add))
            v.tensor_copy(col(31), col(0)).then_inc(mean_ready, 1)
            dve.wait_ge(mean_summed, 1)
            link(v.tensor_copy(col(4), psum[:, 4, 0:1]))
            link(v.tensor_tensor(col(5), col(0), col(4), ALU.subtract))
            link(v.tensor_tensor(col(7), col(5), col(5), ALU.mult))
            v.tensor_tensor(col(6), col(7), col(3), ALU.add).then_inc(spread_ready, 1)
            dve.wait_ge(var_summed, 1)
            v.tensor_scalar_add(col(8), psum[:, 5, 0:1], EPS).then_inc(var_ready, 1)
            dve.wait_ge(std_ready, 1)
            link(v.reciprocal(col(10), col(9)))
            link(v.tensor_tensor(col(11), col(10), col(10), ALU.mult))
            link(v.tensor_tensor(col(12), col(11), col(8), ALU.mult))
            link(v.tensor_scalar(col(13), col(12), -0.5, 1.5, ALU.mult, ALU.add))
            link(v.tensor_tensor(col(14), col(10), col(13), ALU.mult))
            v.scalar_tensor_tensor(col(15), col(4), -1.0, col(14), ALU.mult, ALU.mult).then_inc(scale_ready, 1)
            dve.wait_ge(scale_moved, 1)
            v.tensor_copy(col(16, width=2), psum[:, 6, 0:2])
            v.tensor_copy(col(19, VP), psum[0:VP, 7, 1:2])
            v.tensor_tensor(col(18, VP), psum[0:VP, 7, 0:1], const["unit"][0:VP, :], ALU.mult).then_inc(scale_kept, 1)
            dve.wait_ge(scale_kept, 1)
            for half, w in enumerate((w_lower, w_upper)):
                link(v.tensor_scalar_mul(w, w, col(16)))
                link(v.tensor_tensor(mix[:, half * H:(half + 1) * H].rearrange("p (o q) -> p o q", q=Q),
                                     w.unsqueeze(2).to_broadcast([P, C, Q]),
                                     mask[:, :].unsqueeze(1).to_broadcast([P, C, Q]), ALU.mult))
            link(v.tensor_tensor(mix[:, :], mix[:, :], const["eye"], ALU.add))
            dve.wait_ge(vectors_ready, 1)
            link(v.tensor_scalar_mul(col(20, VP), col(21, VP), 1.0 / N))
            v.tensor_copy(col(20, C, base=V_COL), col(19, C, base=V_COL)).then_inc(means_ready, 1)
            for k in range(LEAD):
                turn(0, 0, k, True, piece_freed=False)
            dve.wait_ge(tables_summed, 1)
            v.tensor_copy(col(22), psum[:, 6, 0:1])
            link(v.tensor_copy(col(23, H), psum[0:H, 7, 0:1]))
            v.tensor_scalar_add(per_row[:, :], psum[:, 4, :], col(22))
            v.tensor_scalar_add(on_diag[:, :], psum[0:H, 5, :], col(23, H))

            def split(j):
                cols = slice(j * BANK, (j + 1) * BANK)
                dve.wait_ge(full_copied, j + 1)
                link(v.tensor_copy(along[:, cols], full[:, cols]))
                link(v.tensor_tensor(full[:, cols], full[:, cols], along[:, cols], ALU.subtract))
                link(v.tensor_copy(middle[:, cols], full[:, cols]))
                v.tensor_copy(along[32:64, cols], middle[32:64, cols])
                v.tensor_tensor(along[64:96, cols], full[64:96, cols], middle[64:96, cols], ALU.subtract).then_inc(along_ready, 1)
                dve.wait_ge(along_ready, j + 1)

            split(0)
            dve.wait_ge(full_copied, 4)
            v.memset(col(60), 0.0).then_inc(evacuated, FREE)
            v.memset(col(61), 0.0).then_inc(taken, FREE)
            v.memset(col(62), 0.0).then_inc(setup_done, 1)

            def add_diagonal(p, k):
                r, _ = block_of(p)
                dve.wait_ge(taken, p * UNITS + (k + FREE))
                v.tensor_tensor(diag_add[:, :, :],
                                on_diag[:, bass.ds(r * M_BLOCK + k * M_UNIT, M_UNIT)].unsqueeze(2).to_broadcast([H, M_UNIT, Q]),
                                mask[0:H, :].unsqueeze(1).to_broadcast([H, M_UNIT, Q]), ALU.mult).then_inc(diag_masked, 1)
                dve.wait_ge(diag_masked, p * UNITS + (k + 1))
                lo = unit_cols(k) + k * M_UNIT * Q
                step = B + Q
                here = result[0:H, lo:lo + M_UNIT * step].rearrange("p (m s) -> p m s", s=step)[:, :, 0:Q]
                v.tensor_tensor(here, here, diag_add[:, :, :], ALU.add).then_inc(taken, 1)

            def turn_back(p, par, k, stored):
                dve.wait_ge(evacuated, p * UNITS + (k + 1 + FREE))
                if k == 0:
                    wait_if(dve, turned_stored[par], stored)
                return v.transpose(unit_strips(turned_out, par, k, 0),
                                   unit_side(result, k, 0).rearrange("p m (b s) -> p m b s", s=32))

            def turn_back_below(p, par, k, stored):
                dve.wait_ge(evacuated, p * UNITS + (k + 1 + FREE))
                if k == 0:
                    wait_if(dve, turned_stored[par], stored)
                c0 = first_col(True, k // 2 + 1)
                if c0 < B:
                    v.transpose(unit_strips(turned_out, par, k, c0 // 32),
                                unit_side(result, k, c0).rearrange("p m (b s) -> p m b s", s=32))

            def ahead(p, par, k, diag, next_diag, last):
                if k + LEAD < UNITS:
                    turn(p, par, k + LEAD, diag)
                elif not last:
                    turn(p + 1, 1 - par, k + LEAD - UNITS, next_diag)

            def finish_block(p, par, stored, diag=False, next_diag=False, last=False):
                for k in range(UNITS):
                    if diag:
                        turn_back_below(p, par, k, stored)
                        add_diagonal(p, k)
                    else:
                        turn_back(p, par, k, stored).then_inc(taken, 1)
                    ahead(p, par, k, diag, next_diag, last)

            for j in range(1, 4):
                split(j)
            finish_block(0, 0, 0, True, True)
            finish_block(1, 1, 0, True, True)
            with dve.Fori(1, DIAG_BLOCKS // 2 - 1) as i:
                finish_block(i * 2, 0, i * DIAG_STRIP_DMAS, True, True)
                finish_block(i * 2 + 1, 1, i * DIAG_STRIP_DMAS, True, True)
            before = DIAG_BLOCKS // 2 * DIAG_STRIP_DMAS
            finish_block(DIAG_BLOCKS - 2, 0, before - DIAG_STRIP_DMAS, True, True)
            finish_block(DIAG_BLOCKS - 1, 1, before - DIAG_STRIP_DMAS, True)
            offset = before - DIAG_BLOCKS // 2 * STRIP_DMAS
            with dve.Fori(DIAG_BLOCKS // 2, BLOCKS // 2 - 1) as i:
                finish_block(i * 2, 0, i * STRIP_DMAS + offset)
                finish_block(i * 2 + 1, 1, i * STRIP_DMAS + offset)
            stored = (BLOCKS // 2 - 1) * STRIP_DMAS + offset
            finish_block(BLOCKS - 2, 0, stored)
            finish_block(BLOCKS - 1, 1, stored, last=True)


def kernel(x, L0_conv_weights, L0_conv_bias):
    import concourse.bacc as bacc
    from concourse.bass_utils import run_bass_kernel_spmd

    nc = bacc.Bacc("TRN2", target_bir_lowering=False, num_devices=1)
    arrays = {
        "in_x": np.ascontiguousarray(x),
        "in_weights": np.ascontiguousarray(L0_conv_weights),
        "in_bias": np.ascontiguousarray(L0_conv_bias),
        "in_consts": constants(),
    }
    aps = {n: nc.dram_tensor(n, a.shape, mybir.dt.from_np(a.dtype), kind="ExternalInput").ap() for n, a in arrays.items()}
    out = nc.dram_tensor("out_0", (1, C, N, N), F32, kind="ExternalOutput").ap()
    program(nc, aps["in_x"].rearrange("a c r s -> (a c) r s"), aps["in_weights"], aps["in_bias"], aps["in_consts"],
            out.rearrange("a c r s -> (a c) r s"))
    r = run_bass_kernel_spmd(nc, [arrays], core_ids=[0])
    return r.results[0]["out_0"]
```

```python
from contextlib import ExitStack

import numpy as np

import concourse.bass as bass
from concourse import mybir
from concourse.alu_op_type import AluOpType as ALU

F32 = mybir.dt.float32
BF16 = mybir.dt.bfloat16
ACT = mybir.ActivationFunctionType
AX_X = mybir.AxisListType.X

P = 128
C = 16
N = 2048
GROUPS = 8
EPS = 1e-5
BANK = 512

ROWS1 = P // C
TILES1 = N // ROWS1
RING1 = 8
PE_COLS = 2 * BANK
POOL_COLS = N - PE_COLS

Q = 4
H = C * Q
B = 256
NB = N // B
M_BLOCK = B // Q
M_UNIT = 8
UNIT = M_UNIT * B
UNITS = M_BLOCK // M_UNIT
PIECE = 2 * UNIT
PIECES = UNITS // 2
SB = B // 32
STRIPS_AT = (range(0, 4), range(4, 6), range(6, 8), ())
C8 = C // 2
BLOCKS = NB + NB * (NB - 1) // 2
DIAG_BLOCKS = NB
PAIR_BLOCKS = BLOCKS - DIAG_BLOCKS
ROWS_PIECE = 2 * M_UNIT * Q
FREE = 2
LEAD = 4
PIECE_DMAS = Q * 16
ALL_DIAGONAL = DIAG_BLOCKS * PIECES // 2 * PIECE_DMAS
ALL_DIRECT = PAIR_BLOCKS * PIECES // 2 * PIECE_DMAS
STRIP_DMAS = SB * 2 * 16
DIAG_STRIP_DMAS = (SB - ROWS_PIECE // 32) * 2 * 16

V_DIAG, V_ROW, V_COL, VP = 0, 32, 64, 96

W_DIRECT, W_TURNED = 8, 6
FEEDS = {
    "A": (5, 12, 7),
    "B": (9, 13, 10),
    "D": (0, 3, 1),
    "K": (11, 14, W_DIRECT),
    "K2": (None, None, W_TURNED),
    "DK": (2, 4, None),
}
SLOTS = list(FEEDS)
SMALL_DMAS = sum(w is not None for f in FEEDS.values() for w in f) + 4 * Q + 1

CONSTS = {"diag_rows": VP, "mean_rows": VP, "column_rows": VP, "none": VP, "group": P, "to_vectors": VP, "to_halves": P,
          "eye": P, "spread": P, "mask": Q, "mask8": ROWS1, "unit": 1}
CONST_COLS = sum(CONSTS.values())


def constants():
    p = np.arange(P)
    c1 = p // ROWS1
    out = {k: np.zeros((P, n), np.float32) for k, n in CONSTS.items()}
    per = P // GROUPS
    out["group"][:] = (p[:, None] // per == p[None, :] // per) / per
    for c in range(C):
        mine = c1 == c
        out["diag_rows"][mine, V_DIAG + c] = 1.0
        out["mean_rows"][mine, V_ROW + c] = 1.0
        out["column_rows"][mine, V_COL + c] = 1.0
        for base in (V_DIAG, V_ROW, V_COL):
            out["to_vectors"][c * ROWS1, base + c] = 1.0
        for half in range(2):
            out["to_halves"][c * ROWS1, half * H + c * Q:half * H + (c + 1) * Q] = 1.0
    out["eye"][p, p] = 1.0
    for part in range(3):
        for which in range(2):
            for o in range(C):
                row = 32 * part + C * which + o
                out["spread"][row, which * H + o * Q:which * H + (o + 1) * Q] = 1.0
    out["mask"][p, p % Q] = 1.0
    out["mask8"][p, p % ROWS1] = 1.0
    out["unit"][:] = 1.0
    out["unit"][V_COL:V_COL + C] = 1.0 / N
    return np.concatenate([out[k] for k in CONSTS], 1)


def program(nc, x, weights, bias, consts, out):
    with ExitStack() as ctx:
        def sb(name, shape, dt=F32):
            return ctx.enter_context(nc.sbuf_tensor(name, shape, dt))

        def sem(name):
            return ctx.enter_context(nc.semaphore(name))

        turned_in = sb("turned_in", [P, SB * C8 * B])
        turned_out = sb("turned_out", [P, SB * C8 * B])
        mixed_in = sb("mixed_in", [P, 2, PIECE])
        result = sb("result", [P, 2 * PIECE + B])
        psum = ctx.enter_context(nc.psum_tensor("psum", [P, 8, BANK], F32))

        mix = sb("mix", [P, P])
        spread = sb("spread", [P, P], BF16)
        along = sb("along", [VP, N], BF16)
        per_row = sb("per_row", [P, N // Q])
        on_diag = sb("on_diag", [H, N // Q])
        along_now = sb("along_now", [VP, 2, B], BF16)
        per_row_now = sb("per_row_now", [P, 2, M_BLOCK])
        mask = sb("mask", [P, Q])
        small = sb("small", [P, 64])
        diag_add = sb("diag_add", [H, M_UNIT, Q])

        tiles = turned_out[:, :].rearrange("p (k n) -> p k n", k=RING1)
        masked_diag = result[:, 0:N]
        masked_mean = result[:, N:2 * N]
        work = result[:, 2 * N:3 * N]
        pool_sum = work[:, 0:POOL_COLS]
        row_stats = work[:, 1024:1536].rearrange("p (t k) -> p t k", k=2)
        chunk_stats = work[:, 1536:1536 + RING1 * 24].rearrange("p (k j f) -> p k j f", k=RING1, f=6)
        ring_stats = work[:, 1792:1792 + 2 * RING1].rearrange("p (k f) -> p k f", f=2)
        vec = turned_out[0:VP, 0:N]
        full = turned_out[0:VP, N:2 * N]
        middle = turned_out[0:VP, 2 * N:2 * N + N // 2].bitcast(BF16)
        at = 3 * N
        const = {}
        for k, n in CONSTS.items():
            const[k] = result[:, at:at + n]
            at += n
        all_consts = result[:, 3 * N:at]

        def table(rows, n):
            nonlocal at
            at += n
            assert at <= 2 * PIECE + B
            return result[0:rows, at - n:at]

        row_mix = table(VP, Q * P).rearrange("p (q n) -> p q n", q=Q)
        diag_mix = table(VP, Q * H).rearrange("p (q n) -> p q n", q=Q)
        along_mix = work[0:VP, 1824:1824 + VP]
        const_mix = table(VP, P)
        const_diag_mix = table(VP, H)
        w_vec = table(VP, len(SLOTS) * C).rearrange("p (k o) -> p k o", o=C)
        w_lower = table(P, C)
        w_upper = table(P, C)
        ones_row = table(P, P)
        bias_col = table(P, 1)

        def col(n, rows=P, width=1, base=0):
            return small[base:base + rows, n:n + width]

        psum_flat = psum[:, :, :].rearrange("p b n -> p (b n)")

        tile_loaded = [sem(f"tile_loaded{k}") for k in range(RING1)]
        rows_read, cols_read, pool_read = sem("rows_read"), sem("cols_read"), sem("pool_read")
        pool_cleared = sem("pool_cleared")
        rows_merged, rows_kept = sem("rows_merged"), sem("rows_kept")
        consts_loaded, weights_loaded = sem("consts_loaded"), sem("weights_loaded")
        zeroed = sem("zeroed")
        dve_step = sem("dve_step")
        vectors_masked, vectors_summed, full_copied = sem("vectors_masked"), sem("vectors_summed"), sem("full_copied")
        along_summed, along_ready = sem("along_summed"), sem("along_ready")
        mean_ready, mean_summed, spread_ready, var_summed = sem("mean_ready"), sem("mean_summed"), sem("spread_ready"), sem("var_summed")
        var_ready, std_ready, scale_ready, scale_moved = sem("var_ready"), sem("std_ready"), sem("scale_ready"), sem("scale_moved")
        vectors_ready, tables_summed, setup_done = sem("vectors_ready"), sem("tables_summed"), sem("setup_done")
        scale_kept, means_ready = sem("scale_kept"), sem("means_ready")
        turned_loaded = [sem(f"turned_loaded{k}") for k in range(2)]
        direct_loaded = [sem(f"direct_loaded{k}") for k in range(2)]
        turned_ready, mixed, evacuated, taken = sem("turned_ready"), sem("mixed"), sem("evacuated"), sem("taken")
        bias_ready, diag_masked = sem("bias_ready"), sem("diag_masked")
        direct_stored = [sem(f"direct_stored{k}") for k in range(2)]
        diagonal_stored = [sem(f"diagonal_stored{k}") for k in range(2)]
        turned_stored = [sem(f"turned_stored{k}") for k in range(2)]

        x_m = x.rearrange("c (m q) s -> c m q s", q=Q)
        out_m = out.rearrange("c (m q) s -> c m q s", q=Q)

        def block_of(p, diag):
            r = p & (NB - 1)
            return (r, r) if diag else (r, (p + (p >> 3) + 1) & (NB - 1))

        def place(eng, p, diag):
            r, s = block_of(p, diag)
            if isinstance(p, int):
                return r, s
            r = eng.snap(eng.to_reg(r))
            return r, r if diag else eng.snap(eng.to_reg(s))

        def half_of(par):
            return H if par == 0 else 0

        def first_col(diag, kk):
            return kk * ROWS_PIECE if diag else 0

        def direct_dram(t, at_block, kk, rr, diag):
            r, s = at_block
            c0 = first_col(diag, kk)
            return t[:, bass.ds(r * M_BLOCK + kk * 2 * M_UNIT, 2 * M_UNIT), rr, bass.ds(s * B + c0, B - c0)]

        def piece_side(t, kk, rr, diag):
            slot = kk % 2
            v = t[rr:H:Q, slot * PIECE:(slot + 1) * PIECE].rearrange("p (m s) -> p m s", s=B)
            return v[:, :, first_col(diag, kk):]

        def strip_width(diag, b, own):
            return (b * 32 // ROWS_PIECE + own) * ROWS_PIECE if diag else B

        def turned_dram(t, at_block, b, h, width):
            r, s = at_block
            return t[h * C8:(h + 1) * C8, bass.ds(s * B + b * 32, 32), bass.ds(r * B, width)].rearrange("c s r -> s c r")

        def strip_side(t, par, b, h, width):
            lo = half_of(par) + 32 * h
            return t[lo:lo + 32, b * C8 * B:(b + 1) * C8 * B].rearrange("p (c r) -> p c r", c=C8)[:, :, 0:width]

        def unit_strips(t, par, k, b0):
            lo = half_of(par)
            v = t[lo:lo + H, :].rearrange("p (b c r) -> p b c r", b=SB, c=C8)
            return v[:, b0:, :, k * M_UNIT * Q:(k + 1) * M_UNIT * Q].rearrange("p b c (m q) -> p m b c q", q=Q)

        def unit_side(t, k, c0):
            lo = unit_cols(k)
            return t[H:P, lo:lo + UNIT].rearrange("p (m s) -> p m s", s=B)[:, :, c0:]

        mixed_flat = mixed_in[:, :, :].rearrange("p k n -> p (k n)")

        def unit_cols(k):
            return ((k // 2) % 2) * PIECE + (k % 2) * UNIT

        def wait_if(eng, semaphore, value):
            if not isinstance(value, int) or value > 0:
                eng.wait_ge(semaphore, value)

        def store_piece(eng, at_block, kk, diag):
            stored = diagonal_stored if diag else direct_stored
            for rr in range(Q):
                eng.dma_start(direct_dram(out_m, at_block, kk, rr, diag),
                              piece_side(result, kk, rr, diag)).then_inc(stored[kk % 2], 16)

        block = ctx.enter_context(nc.Block())

        @block.sync
        def _(sp):
            def load_tile(t, k):
                sp.dma_start(tiles[:, k, :], x[:, bass.ds(t * ROWS1, ROWS1), :]).then_inc(tile_loaded[k], 16)

            load_tile(0, 0)
            sp.dma_start(all_consts, consts).then_inc(consts_loaded, 16)
            for k in range(1, RING1):
                load_tile(k, k)
            with sp.Fori(0, TILES1 // RING1 - 1) as i:
                for k in range(RING1):
                    sp.wait_ge(rows_read, i * RING1 + (k + 1))
                    sp.wait_ge(cols_read, i * RING1 + (k + 1))
                    sp.wait_ge(pool_read, i * RING1 + (k + 1))
                    load_tile(i * RING1 + (RING1 + k), k)

            def load_piece(at_block, kk, diag):
                for rr in range(Q):
                    sp.dma_start(piece_side(mixed_flat, kk, rr, diag),
                                 direct_dram(x_m, at_block, kk, rr, diag)).then_inc(direct_loaded[kk % 2], 16)

            def load_strips(at_block, par, bs, diag):
                for b in bs:
                    w = strip_width(diag, b, 1)
                    for h in range(2):
                        sp.dma_start(strip_side(turned_in, par, b, h, w), turned_dram(x, at_block, b, h, w)).then_inc(turned_loaded[par], 16)

            first = block_of(0, False)
            load_strips(first, 0, range(SB), False)
            load_piece(first, 0, False)
            load_piece(first, 1, False)
            load_strips(block_of(1, False), 1, range(SB), False)

            def block_loads(p, par, diag=False, next_diag=False, last=False):
                here, following = place(sp, p, diag), None if last else place(sp, p + 1, next_diag)
                ahead = not last and not (isinstance(p, int) and p == 0)
                if ahead:
                    wait_if(sp, turned_ready, p * UNITS)
                for kk in range(PIECES):
                    if ahead:
                        load_strips(following, 1 - par, STRIPS_AT[kk], next_diag)
                    if last and kk >= 2:
                        continue
                    sp.wait_ge(mixed, p * UNITS + (2 * kk + 2))
                    if kk < 2:
                        load_piece(here, kk + 2, diag)
                    else:
                        load_piece(following, kk - 2, next_diag)

            block_loads(0, 0)
            block_loads(1, 1)
            with sp.Fori(1, PAIR_BLOCKS // 2 - 1) as i:
                block_loads(i * 2, 0)
                block_loads(i * 2 + 1, 1)
            block_loads(PAIR_BLOCKS - 2, 0)
            block_loads(PAIR_BLOCKS - 1, 1, next_diag=True)
            with sp.Fori(PAIR_BLOCKS // 2, BLOCKS // 2 - 1) as i:
                block_loads(i * 2, 0, True, True)
                block_loads(i * 2 + 1, 1, True, True)
            block_loads(BLOCKS - 2, 0, True, True)
            block_loads(BLOCKS - 1, 1, True, last=True)

        @block.gpsimd
        def _(pool):
            nc.gpsimd.memset(pool_sum, 0.0).then_inc(pool_cleared, 1)
            pool.wait_ge(pool_cleared, 1)

            def sum_columns(i):
                for k in range(RING1):
                    pool.wait_ge(tile_loaded[k], i * 16 + 16)
                    wait_if(pool, pool_read, i * RING1 + k)
                    nc.gpsimd.tensor_tensor(pool_sum, pool_sum, tiles[:, k, PE_COLS:N], ALU.add).then_inc(pool_read, 1)

            sum_columns(0)
            with pool.Fori(1, TILES1 // RING1) as i:
                sum_columns(i)

            def store_strips(at_block, par, bs, diag):
                for b in bs:
                    w = strip_width(diag, b, 0)
                    if w == 0:
                        continue
                    for h in range(2):
                        pool.dma_start(turned_dram(out, at_block, b, h, w), strip_side(turned_out, par, b, h, w)).then_inc(turned_stored[par], 16)

            def diagonal_block_stores(p, par):
                here = place(pool, p, True)
                pool.wait_ge(taken, p * UNITS + (UNITS - 2 + FREE))
                store_strips(here, par, range(SB), True)

            def block_stores(p, par, first=False):
                here = place(pool, p, False)
                if not first:
                    behind = place(pool, p - 1, False)
                    pool.wait_ge(taken, p * UNITS + FREE)
                for kk in range(PIECES):
                    if not first:
                        store_strips(behind, 1 - par, range(3 * kk, min(3 * kk + 3, SB)), False)
                    pool.wait_ge(evacuated, p * UNITS + (2 * kk + 2 + FREE))
                    store_piece(pool, here, kk, False)

            block_stores(0, 0, first=True)
            with pool.Fori(0, PAIR_BLOCKS // 2 - 1) as i:
                block_stores(i * 2 + 1, 1)
                block_stores(i * 2 + 2, 0)
            block_stores(PAIR_BLOCKS - 1, 1)
            pool.wait_ge(taken, PAIR_BLOCKS * UNITS + FREE)
            store_strips(block_of(PAIR_BLOCKS - 1, False), 1, range(SB), False)
            with pool.Fori(PAIR_BLOCKS // 2, BLOCKS // 2) as i:
                diagonal_block_stores(i * 2, 0)
                diagonal_block_stores(i * 2 + 1, 1)
            for slot in range(2):
                pool.wait_ge(diagonal_stored[slot], ALL_DIAGONAL)
                pool.wait_ge(direct_stored[slot], ALL_DIRECT)
                pool.wait_ge(turned_stored[slot], PAIR_BLOCKS // 2 * STRIP_DMAS + DIAG_BLOCKS // 2 * DIAG_STRIP_DMAS)

        @block.scalar
        def _(act):
            act.wait_ge(zeroed, 2)
            for slot, name in enumerate(SLOTS):
                for base, which in zip((V_DIAG, V_ROW, V_COL), FEEDS[name]):
                    if which is not None:
                        act.dma_start(w_vec[base:base + C, slot, :], weights[which]).then_inc(weights_loaded, 16)
            for half, (lower, upper) in enumerate(((W_DIRECT, W_TURNED), (W_TURNED, W_DIRECT))):
                for dst, which in ((w_lower, lower), (w_upper, upper)):
                    for rr in range(Q):
                        act.dma_start(dst[half * H + rr:(half + 1) * H:Q, :], weights[which]).then_inc(weights_loaded, 16)
            act.dma_start(bias_col[0:15, :], bias.rearrange("(p a) -> p a", a=1)).then_inc(weights_loaded, 16)

            act.wait_ge(var_ready, 1)
            nc.scalar.activation(col(9), col(8), ACT.Sqrt).then_inc(std_ready, 1)
            act.wait_ge(vectors_summed, 1)
            act.wait_ge(scale_kept, 1)
            for j in range(4):
                nc.scalar.activation(vec[:, j * BANK:(j + 1) * BANK], psum[0:VP, j, :], ACT.Identity, bias=col(19, VP),
                                     scale=col(18, VP), accum_out=col(40 + j, VP)).then_inc(vectors_ready, 1)
            for j in range(4):
                act.wait_ge(along_summed, j + 1)
                nc.scalar.copy(full[:, j * BANK:(j + 1) * BANK], psum[0:VP, j, :]).then_inc(full_copied, 1)

            def bias_slices(p, par, diag):
                r, s = block_of(p, diag)
                nc.scalar.copy(per_row_now[:, par, :], per_row[:, bass.ds(r * M_BLOCK, M_BLOCK)]).then_inc(bias_ready, 1)
                nc.scalar.copy(along_now[:, par, :], along[:, bass.ds(s * B, B)]).then_inc(bias_ready, 1)

            act.wait_ge(setup_done, 1)
            bias_slices(0, 0, False)

            def store_diagonal_piece(p, kk):
                here = place(act, p, True)
                act.wait_ge(taken, p * UNITS + (2 * kk + 2 + FREE))
                store_piece(act, here, kk, True)

            def evacuate_block(p, par, diag=False, next_diag=False, last=False):
                first_diag = isinstance(p, int) and p == PAIR_BLOCKS
                act.wait_ge(bias_ready, p * 2 + 2)
                for k in range(UNITS):
                    act.wait_ge(mixed, p * UNITS + (k + 1))
                    if k == 1 and isinstance(p, int) and p < 2:
                        act.wait_ge(along_ready, 2 if p == 0 else 4)
                    if k == 1 and not last:
                        act.wait_ge(evacuated, p * UNITS + FREE)
                        bias_slices(p + 1, 1 - par, next_diag)
                    if k % 2 == 0:
                        slot, before = (k // 2) % 2, p * (2 * PIECE_DMAS) + (k // 4) * PIECE_DMAS
                        if not diag:
                            wait_if(act, direct_stored[slot], before)
                        elif first_diag and k < 4:
                            act.wait_ge(direct_stored[slot], ALL_DIRECT)
                        else:
                            act.wait_ge(diagonal_stored[slot], before - ALL_DIRECT)
                        wait_if(act, taken, p * UNITS + k)
                    banks = psum[:, 4 * (k % 2):4 * (k % 2) + 4, :].rearrange("p b (m s) -> p (b m) s", s=B)
                    for m in range(M_UNIT):
                        lo, c0 = unit_cols(k) + m * B, first_col(diag, k // 2)
                        one = nc.scalar.activation(result[:, lo + c0:lo + B], banks[:, m, c0:], ACT.Identity,
                                                   bias=per_row_now[:, par, k * M_UNIT + m:k * M_UNIT + m + 1])
                    one.then_inc(evacuated, 1)
                    if diag and k % 2 == 0:
                        if k > 0:
                            store_diagonal_piece(p, k // 2 - 1)
                        elif not first_diag:
                            store_diagonal_piece(p - 1, PIECES - 1)

            evacuate_block(0, 0)
            evacuate_block(1, 1)
            with act.Fori(1, PAIR_BLOCKS // 2 - 1) as i:
                evacuate_block(i * 2, 0)
                evacuate_block(i * 2 + 1, 1)
            evacuate_block(PAIR_BLOCKS - 2, 0)
            evacuate_block(PAIR_BLOCKS - 1, 1, next_diag=True)
            evacuate_block(PAIR_BLOCKS, 0, True, True)
            with act.Fori(PAIR_BLOCKS // 2, BLOCKS // 2 - 1) as i:
                evacuate_block(i * 2 + 1, 1, True, True)
                evacuate_block(i * 2 + 2, 0, True, True)
            evacuate_block(BLOCKS - 1, 1, True, last=True)
            store_diagonal_piece(BLOCKS - 1, PIECES - 1)

        @block.tensor
        def _(pe):
            pe.wait_ge(consts_loaded, 16)

            def column_sums(i, first=False):
                for k in range(RING1):
                    pe.wait_ge(tile_loaded[k], i * 16 + 16)
                    for j in range(PE_COLS // BANK):
                        one = nc.tensor.matmul(psum[0:VP, j, :], const["column_rows"], tiles[:, k, j * BANK:(j + 1) * BANK],
                                               start=(first and k == 0), stop=False, skip_group_check=True)
                    one.then_inc(cols_read, 1)

            def place_rows(i):
                pe.wait_ge(vectors_masked, i + 1)
                lo = i * (RING1 * ROWS1)
                for name, masked in (("diag_rows", masked_diag), ("mean_rows", masked_mean)):
                    nc.tensor.matmul(psum_flat[0:VP, bass.ds(lo, RING1 * ROWS1)], const[name],
                                     masked[:, bass.ds(lo, RING1 * ROWS1)], start=False, stop=False, skip_group_check=True)

            for j in range(PE_COLS // BANK, 4):
                nc.tensor.matmul(psum[0:VP, j, :], const["none"], all_consts[:, 0:BANK], start=True, stop=False,
                                 skip_group_check=True)
            column_sums(0, first=True)
            with pe.Fori(1, TILES1 // RING1) as i:
                column_sums(i)
                place_rows(i - 1)
            place_rows(TILES1 // RING1 - 1)
            pe.wait_ge(pool_read, TILES1)
            for j in range(PE_COLS // BANK, 4):
                one = nc.tensor.matmul(psum[0:VP, j, :], const["column_rows"],
                                       pool_sum[:, j * BANK - PE_COLS:(j + 1) * BANK - PE_COLS],
                                       start=False, stop=True, skip_group_check=True)
            one.then_inc(vectors_summed, 1)
            pe.wait_ge(mean_ready, 1)
            nc.tensor.matmul(psum[:, 4, 0:1], const["group"], col(0), start=True, stop=True).then_inc(mean_summed, 1)
            pe.wait_ge(spread_ready, 1)
            nc.tensor.matmul(psum[:, 5, 0:1], const["group"], col(6), start=True, stop=True).then_inc(var_summed, 1)
            pe.wait_ge(scale_ready, 1)
            nc.tensor.matmul(psum[:, 6, 0:2], const["to_halves"], col(14, width=2), start=True, stop=True)
            nc.tensor.matmul(psum[0:VP, 7, 0:2], const["to_vectors"], col(14, width=2), start=True, stop=True).then_inc(scale_moved, 1)

            vec_m = vec.rearrange("p (m q) -> p q m", q=Q)
            for j in range(4):
                pe.wait_ge(vectors_ready, j + 1)
                nc.tensor.matmul(psum[0:VP, j, :], along_mix, vec[:, j * BANK:(j + 1) * BANK],
                                 start=True, stop=True).then_inc(along_summed, 1)
            pe.wait_ge(scale_kept, 1)
            for rr in range(Q):
                nc.tensor.matmul(psum[:, 4, :], row_mix[:, rr, :], vec_m[:, rr, :], start=(rr == 0), stop=(rr == Q - 1))
            for rr in range(Q):
                nc.tensor.matmul(psum[0:H, 5, :], diag_mix[:, rr, :], vec_m[:, rr, :], start=(rr == 0), stop=(rr == Q - 1))
            pe.wait_ge(means_ready, 1)
            nc.tensor.matmul(psum[:, 6, 0:1], const_mix, col(20, VP), start=True, stop=False)
            nc.tensor.matmul(psum[:, 6, 0:1], ones_row, bias_col, start=False, stop=True)
            nc.tensor.matmul(psum[0:H, 7, 0:1], const_diag_mix, col(20, VP), start=True, stop=True).then_inc(tables_summed, 1)

            def mix_block(p, par, diag=False):
                for k in range(UNITS):
                    if k % 2 == 0:
                        pe.wait_ge(direct_loaded[(k // 2) % 2], p * (2 * PIECE_DMAS) + (k // 4 + 1) * PIECE_DMAS)
                    pe.wait_ge(turned_ready, p * UNITS + (k + 1))
                    pe.wait_ge(evacuated, p * UNITS + (k + 1))
                    c0 = first_col(diag, k // 2)
                    units_m = BANK // B
                    banks = [psum[:, 4 * (k % 2) + j, :].rearrange("p (m s) -> p m s", s=B)[:, :, c0:] for j in range(4)]
                    for j in range(4):
                        lo = unit_cols(k) + j * BANK
                        nc.tensor.matmul(banks[j], mix[:, :],
                                         mixed_flat[:, lo:lo + BANK].rearrange("p (m s) -> p m s", s=B)[:, :, c0:],
                                         start=True, stop=False, skip_group_check=True)
                    if k == 0:
                        pe.wait_ge(bias_ready, p * 2 + 2)
                    for j in range(4):
                        one = nc.tensor.matmul(banks[j], spread[0:VP, :],
                                               along_now[:, par, c0:].unsqueeze(1).to_broadcast([VP, units_m, B - c0]),
                                               start=False, stop=True, skip_group_check=True)
                    one.then_inc(mixed, 1)

            with pe.Fori(0, PAIR_BLOCKS // 2) as i:
                mix_block(i * 2, 0)
                mix_block(i * 2 + 1, 1)
            with pe.Fori(PAIR_BLOCKS // 2, BLOCKS // 2) as i:
                mix_block(i * 2, 0, True)
                mix_block(i * 2 + 1, 1, True)

        @block.vector
        def _(dve):
            v = nc.vector
            steps = [0]

            def link(ins):
                steps[0] += 1
                ins.then_inc(dve_step, 1)
                dve.wait_ge(dve_step, steps[0])

            v.memset(w_vec, 0.0).then_inc(zeroed, 1)
            v.memset(bias_col, 0.0).then_inc(zeroed, 1)
            v.memset(ones_row, 1.0)
            v.memset(diag_mix, 0.0)
            link(v.memset(row_mix, 0.0))

            dve.wait_ge(consts_loaded, 16)

            def row_statistics(i):
                for k in range(RING1):
                    dve.wait_ge(tile_loaded[k], i * 16 + 16)
                    for j in range(4):
                        v.bn_stats(chunk_stats[:, k, j, :], tiles[:, k, j * BANK:(j + 1) * BANK])
                    here = bass.ds(i * (RING1 * ROWS1) + k * ROWS1, ROWS1)
                    v.tensor_tensor(masked_diag[:, here], tiles[:, k, here], const["mask8"], ALU.mult).then_inc(rows_read, 1)
                dve.wait_ge(rows_read, i * RING1 + RING1)
                v.memset(col(63), 0.0)
                for k in range(RING1):
                    one = v.bn_aggr(ring_stats[:, k, :], chunk_stats[:, k, :, :])
                one.then_inc(rows_merged, 1)
                dve.wait_ge(rows_merged, i + 1)
                v.tensor_copy(row_stats[:, bass.ds(i * RING1, RING1), :], ring_stats[:, :, :]).then_inc(rows_kept, 1)
                v.tensor_tensor(masked_mean[:, bass.ds(i * (RING1 * ROWS1), RING1 * ROWS1)].rearrange("p (k r) -> p k r", r=ROWS1),
                                ring_stats[:, :, 0].unsqueeze(2).to_broadcast([P, RING1, ROWS1]),
                                const["mask8"].unsqueeze(1).to_broadcast([P, RING1, ROWS1]),
                                ALU.mult).then_inc(vectors_masked, 1)
                dve.wait_ge(vectors_masked, i + 1)

            row_statistics(0)

            dve.wait_ge(weights_loaded, SMALL_DMAS * 16)
            slot_of = {name: w_vec[:, n, :] for n, name in enumerate(SLOTS)}
            for rr in range(Q):
                v.tensor_copy(row_mix[:, rr, rr:H:Q], slot_of["A"])
                v.tensor_copy(row_mix[:, rr, H + rr:P:Q], slot_of["B"])
                v.tensor_copy(diag_mix[:, rr, rr:H:Q], slot_of["D"])
            for part in range(3):
                v.tensor_copy(along_mix[:, 32 * part:32 * part + C], slot_of["B"])
                v.tensor_copy(along_mix[:, 32 * part + C:32 * part + 2 * C], slot_of["A"])
            link(v.tensor_tensor(slot_of["K"], slot_of["K"], slot_of["K2"], ALU.add))
            for half in range(2):
                v.tensor_copy(const_mix[:, half * H:(half + 1) * H].rearrange("p (o q) -> p o q", q=Q),
                              slot_of["K"].unsqueeze(2).to_broadcast([VP, C, Q]))
            v.tensor_copy(const_diag_mix.rearrange("p (o q) -> p o q", q=Q),
                          slot_of["DK"].unsqueeze(2).to_broadcast([VP, C, Q]))
            v.tensor_copy(spread[:, :], const["spread"])
            link(v.tensor_copy(mask[:, :], const["mask"]))

            with dve.Fori(1, TILES1 // RING1) as i:
                row_statistics(i)

            def turn(p, par, k, diag, piece_freed=True):
                if k == 0:
                    dve.wait_ge(turned_loaded[par], p * (STRIP_DMAS // 2) + (STRIP_DMAS // 2 * (2 - par)))
                if k % 2 == 0 and piece_freed:
                    dve.wait_ge(mixed, p * UNITS + k - 2)
                c0 = first_col(diag, k // 2)
                v.transpose(unit_side(mixed_flat, k, c0).rearrange("p m (b s) -> p m b s", s=32),
                            unit_strips(turned_in, par, k, c0 // 32)).then_inc(turned_ready, 1)

            dve.wait_ge(rows_kept, TILES1 // RING1)
            link(v.bn_stats(col(24, width=6), row_stats[:, :, 0]))
            link(v.bn_aggr(col(0, width=2), col(24, width=6)))
            link(v.tensor_reduce(col(2), row_stats[:, :, 1], AX_X, ALU.add))
            link(v.scalar_tensor_tensor(col(3), col(2), 1.0 / TILES1, col(1), ALU.mult, ALU.add))
            v.tensor_copy(col(31), col(0)).then_inc(mean_ready, 1)
            dve.wait_ge(mean_summed, 1)
            link(v.tensor_copy(col(4), psum[:, 4, 0:1]))
            link(v.tensor_tensor(col(5), col(0), col(4), ALU.subtract))
            link(v.tensor_tensor(col(7), col(5), col(5), ALU.mult))
            v.tensor_tensor(col(6), col(7), col(3), ALU.add).then_inc(spread_ready, 1)
            dve.wait_ge(var_summed, 1)
            v.tensor_scalar_add(col(8), psum[:, 5, 0:1], EPS).then_inc(var_ready, 1)
            dve.wait_ge(std_ready, 1)
            link(v.reciprocal(col(10), col(9)))
            link(v.tensor_tensor(col(11), col(10), col(10), ALU.mult))
            link(v.tensor_tensor(col(12), col(11), col(8), ALU.mult))
            link(v.tensor_scalar(col(13), col(12), -0.5, 1.5, ALU.mult, ALU.add))
            link(v.tensor_tensor(col(14), col(10), col(13), ALU.mult))
            v.scalar_tensor_tensor(col(15), col(4), -1.0, col(14), ALU.mult, ALU.mult).then_inc(scale_ready, 1)
            dve.wait_ge(scale_moved, 1)
            v.tensor_copy(col(16, width=2), psum[:, 6, 0:2])
            v.tensor_copy(col(19, VP), psum[0:VP, 7, 1:2])
            v.tensor_tensor(col(18, VP), psum[0:VP, 7, 0:1], const["unit"][0:VP, :], ALU.mult).then_inc(scale_kept, 1)
            dve.wait_ge(scale_kept, 1)
            for half, w in enumerate((w_lower, w_upper)):
                link(v.tensor_scalar_mul(w, w, col(16)))
                link(v.tensor_tensor(mix[:, half * H:(half + 1) * H].rearrange("p (o q) -> p o q", q=Q),
                                     w.unsqueeze(2).to_broadcast([P, C, Q]),
                                     mask[:, :].unsqueeze(1).to_broadcast([P, C, Q]), ALU.mult))
            link(v.tensor_tensor(mix[:, :], mix[:, :], const["eye"], ALU.add))
            dve.wait_ge(vectors_ready, 4)
            link(v.tensor_reduce(col(21, VP), col(40, VP, 4), AX_X, ALU.add))
            link(v.tensor_scalar_mul(col(20, VP), col(21, VP), 1.0 / N))
            v.tensor_copy(col(20, C, base=V_COL), col(19, C, base=V_COL)).then_inc(means_ready, 1)

            def split(j):
                cols = slice(j * BANK, (j + 1) * BANK)
                dve.wait_ge(full_copied, j + 1)
                link(v.tensor_copy(along[:, cols], full[:, cols]))
                link(v.tensor_tensor(full[:, cols], full[:, cols], along[:, cols], ALU.subtract))
                link(v.tensor_copy(middle[:, cols], full[:, cols]))
                v.tensor_copy(along[32:64, cols], middle[32:64, cols])
                v.tensor_tensor(along[64:96, cols], full[64:96, cols], middle[64:96, cols], ALU.subtract).then_inc(along_ready, 1)
                dve.wait_ge(along_ready, j + 1)

            def turn_first(k):
                turn(0, 0, k, False, piece_freed=False)

            turn_first(0)
            split(0)
            split(1)
            dve.wait_ge(full_copied, 4)
            v.memset(col(60), 0.0).then_inc(evacuated, 1)
            for k in range(1, LEAD):
                turn_first(k)
            dve.wait_ge(tables_summed, 1)
            v.tensor_copy(col(22), psum[:, 6, 0:1])
            link(v.tensor_copy(col(23, H), psum[0:H, 7, 0:1]))
            v.tensor_scalar_add(per_row[:, :], psum[:, 4, :], col(22))
            v.tensor_scalar_add(on_diag[:, :], psum[0:H, 5, :], col(23, H)).then_inc(evacuated, 1)
            v.memset(col(61), 0.0).then_inc(taken, FREE)
            v.memset(col(62), 0.0).then_inc(setup_done, 1)

            def add_diagonal(p, k):
                r, _ = block_of(p, True)
                dve.wait_ge(taken, p * UNITS + (k + FREE))
                v.tensor_tensor(diag_add[:, :, :],
                                on_diag[:, bass.ds(r * M_BLOCK + k * M_UNIT, M_UNIT)].unsqueeze(2).to_broadcast([H, M_UNIT, Q]),
                                mask[0:H, :].unsqueeze(1).to_broadcast([H, M_UNIT, Q]), ALU.mult).then_inc(diag_masked, 1)
                dve.wait_ge(diag_masked, p * UNITS + (k + 1 - PAIR_BLOCKS * UNITS))
                lo = unit_cols(k) + k * M_UNIT * Q
                step = B + Q
                here = result[0:H, lo:lo + M_UNIT * step].rearrange("p (m s) -> p m s", s=step)[:, :, 0:Q]
                v.tensor_tensor(here, here, diag_add[:, :, :], ALU.add).then_inc(taken, 1)

            def turn_back(p, par, k, stored):
                dve.wait_ge(evacuated, p * UNITS + (k + 1 + FREE))
                if k == 0:
                    wait_if(dve, turned_stored[par], stored)
                return v.transpose(unit_strips(turned_out, par, k, 0),
                                   unit_side(result, k, 0).rearrange("p m (b s) -> p m b s", s=32))

            def turn_back_below(p, par, k, stored):
                dve.wait_ge(evacuated, p * UNITS + (k + 1 + FREE))
                if k == 0:
                    wait_if(dve, turned_stored[par], stored)
                c0 = first_col(True, k // 2 + 1)
                if c0 < B:
                    v.transpose(unit_strips(turned_out, par, k, c0 // 32),
                                unit_side(result, k, c0).rearrange("p m (b s) -> p m b s", s=32))

            def ahead(p, par, k, diag, next_diag, last):
                if k + LEAD < UNITS:
                    turn(p, par, k + LEAD, diag)
                elif not last:
                    turn(p + 1, 1 - par, k + LEAD - UNITS, next_diag)

            def finish_block(p, par, stored, diag=False, next_diag=False, last=False):
                for k in range(UNITS):
                    if diag:
                        turn_back_below(p, par, k, stored)
                        add_diagonal(p, k)
                    else:
                        turn_back(p, par, k, stored).then_inc(taken, 1)
                    ahead(p, par, k, diag, next_diag, last)

            split(2)
            split(3)
            finish_block(0, 0, 0)
            finish_block(1, 1, 0)
            with dve.Fori(1, PAIR_BLOCKS // 2 - 1) as i:
                finish_block(i * 2, 0, i * STRIP_DMAS)
                finish_block(i * 2 + 1, 1, i * STRIP_DMAS)
            stored = PAIR_BLOCKS // 2 * STRIP_DMAS
            finish_block(PAIR_BLOCKS - 2, 0, stored - STRIP_DMAS)
            finish_block(PAIR_BLOCKS - 1, 1, stored - STRIP_DMAS, next_diag=True)
            offset = stored - PAIR_BLOCKS // 2 * DIAG_STRIP_DMAS
            with dve.Fori(PAIR_BLOCKS // 2, BLOCKS // 2 - 1) as i:
                finish_block(i * 2, 0, i * DIAG_STRIP_DMAS + offset, True, True)
                finish_block(i * 2 + 1, 1, i * DIAG_STRIP_DMAS + offset, True, True)
            stored = (BLOCKS // 2 - 1) * DIAG_STRIP_DMAS + offset
            finish_block(BLOCKS - 2, 0, stored, True, True)
            finish_block(BLOCKS - 1, 1, stored, True, last=True)


def kernel(x, L0_conv_weights, L0_conv_bias):
    import concourse.bacc as bacc
    from concourse.bass_utils import run_bass_kernel_spmd

    nc = bacc.Bacc("TRN2", target_bir_lowering=False, num_devices=1)
    arrays = {
        "in_x": np.ascontiguousarray(x),
        "in_weights": np.ascontiguousarray(L0_conv_weights),
        "in_bias": np.ascontiguousarray(L0_conv_bias),
        "in_consts": constants(),
    }
    aps = {n: nc.dram_tensor(n, a.shape, mybir.dt.from_np(a.dtype), kind="ExternalInput").ap() for n, a in arrays.items()}
    out = nc.dram_tensor("out_0", (1, C, N, N), F32, kind="ExternalOutput").ap()
    program(nc, aps["in_x"].rearrange("a c r s -> (a c) r s"), aps["in_weights"], aps["in_bias"], aps["in_consts"],
            out.rearrange("a c r s -> (a c) r s"))
    r = run_bass_kernel_spmd(nc, [arrays], core_ids=[0])
    return r.results[0]["out_0"]
```
